# Optimizing a Trainium2 kernel written in Bass

```python
import numpy as np
import jax
import jax.numpy as jnp

def _softmax(x, axis=-1):
    return jax.nn.softmax(x, axis=axis)

def _gelu(x):
    return jax.nn.gelu(x, approximate=True)

def _silu(x):
    return jax.nn.silu(x)

def _sigmoid(x):
    return jax.nn.sigmoid(x)

def _layernorm(x, axis=-1, eps=1e-05):
    m = jnp.mean(x, axis=axis, keepdims=True)
    v = jnp.var(x, axis=axis, keepdims=True)
    return (x - m) / jnp.sqrt(v + eps)

def _scatter_add(tgt, idx, src, axis=0):
    return tgt.at[idx].add(src)

def _segment_sum(src, seg, n):
    return jax.ops.segment_sum(src, seg, n)
kernel_name = 'mk_seq_preln_d1_jaxref_r8_eccf03'

def setup_inputs(seed: int=0):
    np.random.seed(seed)
    _w = jnp.asarray

    def _L0_attn_setup():
        import jax, jax.numpy as jnp
        import numpy as np
        BATCH, SEQ, HIDDEN = (2, 512, 512)
        HEADS, HEAD_DIM, BLOCK = (32, 128, 32)
        LAYER_IDX, N_LAYERS = (1, 32)
        EPS = 1e-05

        def _decays():
            base = 1.0 / 2.0 ** (8.0 / HEADS)
            exponent = jnp.arange(HEADS, dtype=jnp.float32) + 1.0
            factor = 1.0 - LAYER_IDX / (N_LAYERS - 1 + 1e-05) + 1e-05
            slope = (base ** exponent * factor)[:, None, None]
            r = jnp.arange(BLOCK, dtype=jnp.float32) + 1.0
            q_decay = jnp.exp(-slope * r[:, None])
            k_decay = jnp.exp(-slope * (BLOCK - r)[:, None])
            diff = r[:, None] - r[None, :]
            diag = slope[None] * diff[None, None]
            diag = jnp.where(diag >= 0, -diag, -jnp.inf)
            diag_decay = jnp.exp(diag)
            block_decay = jnp.exp(-slope * BLOCK)
            return (q_decay, k_decay, diag_decay, block_decay)
        key = jax.random.key(seed)
        ks = jax.random.split(key, 5)
        s = 0.02
        return {'hidden_states': jax.random.normal(ks[0], (BATCH, SEQ, HIDDEN), jnp.float32), 'qkv_w': jax.random.normal(ks[1], (3 * HEADS * HEAD_DIM, HIDDEN), jnp.float32) * s, 'out_w': jax.random.normal(ks[2], (HIDDEN, HEADS * HEAD_DIM), jnp.float32) * s, 'gate_w': jax.random.normal(ks[3], (HEADS * HEAD_DIM, HIDDEN), jnp.float32) * s, 'norm_w': jnp.ones((HEADS * HEAD_DIM,), jnp.float32)}
    _L0_attn_in = _L0_attn_setup()

    def _L0_ffn_setup():
        import jax, jax.numpy as jnp
        import numpy as np
        TOP_K = 2
        key = jax.random.key(seed)
        k0, k1, k2 = jax.random.split(key, 3)
        B, S, D, H, E = (4, 256, 512, 512, 8)
        sc = 1.0 / np.sqrt(D).astype(np.float32)
        x = jax.random.normal(k0, (B, S, D), dtype=jnp.float32)
        W_gate = jax.random.normal(k1, (D, E), dtype=jnp.float32) * sc
        b_gate = jnp.zeros((E,), dtype=jnp.float32)
        W_e = jax.random.normal(k2, (E, D, H), dtype=jnp.float32) * sc
        b_e = jnp.zeros((E, H), dtype=jnp.float32)
        return {'x': x, 'W_gate': W_gate, 'b_gate': b_gate, 'W_e': W_e, 'b_e': b_e}
    _L0_ffn_in = _L0_ffn_setup()
    _d = {'L0_attn_hidden_states': _L0_attn_in['hidden_states'], 'L0_attn_qkv_w': _L0_attn_in['qkv_w'], 'L0_attn_out_w': _L0_attn_in['out_w'], 'L0_attn_gate_w': _L0_attn_in['gate_w'], 'L0_attn_norm_w': _L0_attn_in['norm_w'], 'L0_ffn_W_gate': _L0_ffn_in['W_gate'], 'L0_ffn_b_gate': _L0_ffn_in['b_gate'], 'L0_ffn_W_e': _L0_ffn_in['W_e'], 'L0_ffn_b_e': _L0_ffn_in['b_e']}
    _x0 = _d['L0_attn_hidden_states']
    _d['L0_attn_hidden_states'] = jax.random.normal(jax.random.fold_in(jax.random.key(seed), 1), (1, 1024, 512), dtype=_x0.dtype)
    del _x0
    return _d

def reference(L0_attn_hidden_states, L0_attn_qkv_w, L0_attn_out_w, L0_attn_gate_w, L0_attn_norm_w, L0_ffn_W_gate, L0_ffn_b_gate, L0_ffn_W_e, L0_ffn_b_e):

    def _L0_attn_ref(hidden_states, qkv_w, out_w, gate_w, norm_w):
        import jax, jax.numpy as jnp
        import numpy as np
        BATCH, SEQ, HIDDEN = (2, 512, 512)
        HEADS, HEAD_DIM, BLOCK = (32, 128, 32)
        LAYER_IDX, N_LAYERS = (1, 32)
        EPS = 1e-05

        def _decays():
            base = 1.0 / 2.0 ** (8.0 / HEADS)
            exponent = jnp.arange(HEADS, dtype=jnp.float32) + 1.0
            factor = 1.0 - LAYER_IDX / (N_LAYERS - 1 + 1e-05) + 1e-05
            slope = (base ** exponent * factor)[:, None, None]
            r = jnp.arange(BLOCK, dtype=jnp.float32) + 1.0
            q_decay = jnp.exp(-slope * r[:, None])
            k_decay = jnp.exp(-slope * (BLOCK - r)[:, None])
            diff = r[:, None] - r[None, :]
            diag = slope[None] * diff[None, None]
            diag = jnp.where(diag >= 0, -diag, -jnp.inf)
            diag_decay = jnp.exp(diag)
            block_decay = jnp.exp(-slope * BLOCK)
            return (q_decay, k_decay, diag_decay, block_decay)
        b, s, _ = hidden_states.shape
        h, d, bs = (HEADS, HEAD_DIM, BLOCK)
        nb = s // bs
        q_decay, k_decay, diag_decay, block_decay = _decays()
        qkv = jax.nn.silu(hidden_states @ qkv_w.T)
        qkv = qkv.reshape(b, s, h, 3, d)
        q = jnp.moveaxis(qkv[:, :, :, 0], 2, 1)
        k = jnp.moveaxis(qkv[:, :, :, 1], 2, 1)
        v = jnp.moveaxis(qkv[:, :, :, 2], 2, 1)

        def to_blocks(x):
            return jnp.moveaxis(x.reshape(b, h, nb, bs, d), 2, 0)
        qb, kb, vb = (to_blocks(q), to_blocks(k), to_blocks(v))

        def step(kv, blk):
            cq, ck, cv = blk
            scores = jnp.einsum('bhnd,bhmd->bhnm', cq, ck) * diag_decay
            intra = jnp.einsum('bhnm,bhmd->bhnd', scores, cv)
            inter = jnp.einsum('bhnd,bhde->bhne', cq * q_decay, kv)
            kv_next = kv * block_decay + jnp.einsum('bhnd,bhne->bhde', ck * k_decay, cv)
            return (kv_next, intra + inter)
        kv0 = jnp.zeros((b, h, d, d), hidden_states.dtype)
        _, out_blocks = jax.lax.scan(step, kv0, (qb, kb, vb))
        attn = jnp.moveaxis(out_blocks, 0, 2)
        attn = attn.reshape(b, h, s, d).transpose(0, 2, 1, 3).reshape(b, s, h * d)
        xf = attn.astype(jnp.float32)
        xf = xf * jax.lax.rsqrt(jnp.mean(xf * xf, axis=-1, keepdims=True) + EPS)
        normed = norm_w * xf.astype(attn.dtype)
        gate = jax.nn.sigmoid(hidden_states @ gate_w.T)
        return gate * normed @ out_w.T

    def _L0_ffn_ref(x, W_gate, b_gate, W_e, b_e):
        import jax, jax.numpy as jnp
        import numpy as np
        TOP_K = 2
        logits = x @ W_gate + b_gate
        _, top_idx = jax.lax.top_k(logits, TOP_K)
        y_all = jax.nn.relu(jnp.einsum('bsd,edh->bseh', x, W_e) + b_e)
        y = jnp.take_along_axis(y_all, top_idx[..., None], axis=2)
        return y.mean(axis=2)
    x = L0_attn_hidden_states
    x = x + _L0_attn_ref(_layernorm(x, axis=-1), L0_attn_qkv_w, L0_attn_out_w, L0_attn_gate_w, L0_attn_norm_w)
    x = x + _L0_ffn_ref(_layernorm(x, axis=-1), L0_ffn_W_gate, L0_ffn_b_gate, L0_ffn_W_e, L0_ffn_b_e)
    return x

_drawn_inputs = setup_inputs


def setup_inputs(seed=0):
    import zlib

    import numpy as np

    out = dict(_drawn_inputs(seed))
    spreads = {'L0_attn_norm_w': (1.0, 0.2), 'L0_ffn_b_gate': (0.0, 0.1), 'L0_ffn_b_e': (0.0, 0.1)}
    factors = {}
    for name, (base, spread) in spreads.items():
        noise = np.random.default_rng([zlib.crc32(name.encode()), seed]).standard_normal(out[name].shape)
        drawn = base * np.exp(spread * noise) if base else spread * noise
        out[name] = jnp.asarray(drawn.astype(out[name].dtype))
    for name, factor in factors.items():
        out[name] = (out[name] * factor).astype(out[name].dtype)
    return out
```

```python
from contextlib import ExitStack

import numpy as np

import concourse.bass as bass
from concourse import mybir
from concourse.alu_op_type import AluOpType as ALU

F32 = mybir.dt.float32
F32R = mybir.dt.float32r
ACT = mybir.ActivationFunctionType
AX_X = mybir.AxisListType.X

P = 128
TOKENS, HID = 1024, 512
HEADS, HD = 32, 128
EXPERTS, TOP_K = 8, 2
EPS = 1e-5
TILES = TOKENS // P
HC = HID // P
HALF = TOKENS // 2
WCOLS = 3 * HD + 2 * HD
V0 = 3 * HD
BANKS = 6
ORDER = [("q", 0), ("k", 0), ("q", 1), ("k", 1), ("g", 0), ("g", 1)]
COL = {"q": 0, "k": HD, "g": 2 * HD}
PIECES = BANKS * HC // TILES
MASK, QD, KD, BD, NW = 0, HD, 2 * HD, 2 * HD + 1, 2 * HD + 2
CCOLS = 2 * HD + 3
KVN = TILES - 1
LAST = HEADS + 2
FIRST = 4


class Phase:

    def __init__(self, base, reg=None):
        self.base, self.reg, self.half = base, reg, base % 2

    def times(self, n, plus=0):
        c = n * self.base + plus
        return c if self.reg is None else self.reg * (2 * n) + c

    def pair(self, n, plus=0):
        c = n * (self.base // 2) + plus
        return c if self.reg is None else self.reg * n + c

    def flags(self):
        if self.reg is not None:
            return True, True, self.half == 1, True
        g = self.base
        return 1 <= g <= HEADS, g < HEADS, self.half == 1 and g >= 3, g >= 2


def need(eng, semaphore, value):
    if not isinstance(value, int) or value > 0:
        eng.wait_ge(semaphore, value)


def layer(nc, x, weights, experts, head_consts, w_gate, b_gate, b_exp, tri, out):
    with ExitStack() as ctx:
        def sb(name, shape, dt=F32):
            return ctx.enter_context(nc.sbuf_tensor(name, shape, dt))

        def psum(name):
            return ctx.enter_context(nc.psum_tensor(name, [P, 512], F32))

        def sem(name):
            return ctx.enter_context(nc.semaphore(name))

        xs = sb("xs", [P, TILES, HID])
        yacc = sb("yacc", [P, TILES, HID])
        xh = sb("xh", [P, HC, TOKENS], F32R)
        xl = sb("xl", [P, HC, TOKENS], F32R)
        raw = [sb(f"raw{j}", [P, HC, WCOLS]) for j in range(2)]
        wh = [sb(f"wh{j}", [P, HC, WCOLS], F32R) for j in range(2)]
        wl = [sb(f"wl{j}", [P, HC, WCOLS], F32R) for j in range(2)]
        qT = [sb(f"qT{j}", [P, TOKENS]) for j in range(2)]
        kT = [sb(f"kT{j}", [P, TOKENS]) for j in range(2)]
        gT = [sb(f"gT{j}", [P, TOKENS]) for j in range(2)]
        qdT = [sb(f"qdT{j}", [P, TOKENS]) for j in range(2)]
        v = sb("v", [P, TILES, 2 * HD])
        cst = [sb(f"cst{j}", [P, CCOLS]) for j in range(2)]
        kn = sb("kn", [P, HD])
        pm = sb("pm", [P, P])
        kv = [sb(f"kv{j}", [P, HD]) for j in range(2)]
        sq = [sb(f"sq{j}", [P, HALF]) for j in range(2)]
        gt = [sb(f"gt{j}", [P, HALF]) for j in range(2)]
        gh = [sb(f"gh{j}", [P, TOKENS], F32R) for j in range(2)]
        gl = [sb(f"gl{j}", [P, TOKENS], F32R) for j in range(2)]
        sqacc = sb("sqacc", [P, TOKENS])
        ident = sb("ident", [P, P])
        ones = sb("ones", [P, 2])
        stats = sb("stats", [P, TILES, 6])
        mv = sb("mv", [P, TILES, 2])
        var = sb("var", [P, TILES])
        root = sb("root", [P, TILES])
        inv = sb("inv", [P, TILES])
        tmp = sb("tmp", [P, TILES])
        rstd = sb("rstd", [P, TILES])
        wg = sb("wg", [P, HC, EXPERTS])
        wgh = sb("wgh", [P, HC, EXPERTS], F32R)
        wgl = sb("wgl", [P, HC, EXPERTS], F32R)
        bg = sb("bg", [P, EXPERTS])
        tri_sb = sb("tri_sb", [P, EXPERTS, EXPERTS])
        lg = sb("lg", [P, TILES, EXPERTS])
        more = sb("more", [P, EXPERTS, EXPERTS])
        same = sb("same", [P, EXPERTS, EXPERTS])
        rank = sb("rank", [P, TILES, EXPERTS])
        route = sb("route", [P, EXPERTS, TILES])
        bias = [v[:, 2 * j:2 * j + 2, :].rearrange("p a b -> p (a b)") for j in range(2)]
        z, relu = gt, sq

        ps_proj = [psum(f"ps_proj{j}") for j in range(2)]
        ps_vo = psum("ps_vo")
        ps_t = psum("ps_t")
        ps_s = psum("ps_s")
        ps_kv = psum("ps_kv")
        ps_o = [psum(f"ps_o{j}") for j in range(2)]
        ps_ffn = ps_proj + ps_o

        x_in = [sem(f"x_in{t}") for t in range(TILES)]
        raw_in = [sem(f"raw_in{j}") for j in range(2)]
        cst_in = [sem(f"cst_in{j}") for j in range(2)]
        small_in = sem("small_in")
        bias_in = [sem(f"bias_in{j}") for j in range(2)]
        out_sent = sem("out_sent")
        ident_made = sem("ident_made")
        zeroed = sem("zeroed")
        yacc_zeroed = sem("yacc_zeroed")
        var_ready = sem("var_ready")
        root_ready = sem("root_ready")
        xn_ready = sem("xn_ready")
        xt_done = sem("xt_done")
        xh_ready = sem("xh_ready")
        xl_ready = sem("xl_ready")
        w_hi = [sem(f"w_hi{j}") for j in range(2)]
        w_lo = [sem(f"w_lo{j}") for j in range(2)]
        wg_hi = sem("wg_hi")
        wg_lo = sem("wg_lo")
        proj_done = sem("proj_done")
        proj_ready = sem("proj_ready")
        qd_ready = sem("qd_ready")
        v_done = sem("v_done")
        v_ready = sem("v_ready")
        t_done = sem("t_done")
        kn_ready = sem("kn_ready")
        s_done = sem("s_done")
        pm_ready = sem("pm_ready")
        kv_done = sem("kv_done")
        kv_ready = sem("kv_ready")
        o_done = sem("o_done")
        sq_ready = sem("sq_ready")
        sq_added = sem("sq_added")
        gt_ready = sem("gt_ready")
        gh_ready = sem("gh_ready")
        gl_ready = sem("gl_ready")
        y_done = sem("y_done")
        y_added = sem("y_added")
        rms_done = sem("rms_done")
        logit_done = sem("logit_done")
        routed = sem("routed")
        f_done = sem("f_done")
        z_ready = sem("z_ready")
        relu_ready = sem("relu_ready")
        f_added = sem("f_added")
        step = sem("step")

        block = ctx.enter_context(nc.Block())
        GROUP = 2
        GROUPS = TILES // GROUP
        SPLITS = HC * (LAST // 2)

        def expert_splits(e):
            return SPLITS + HC * (e // 2 + e % 2)

        def loop(engine):
            return nc.Fori(0, (HEADS - FIRST) // 2, engines=[engine], hint_back_edge=True)

        @block.sync
        def _(sp):
            for t in range(TILES):
                sp.dma_start(xs[:, t, :], x[t * P:(t + 1) * P, :]).then_inc(x_in[t], 16)
            sp.dma_start(raw[0][:, :, :], weights[0]).then_inc(raw_in[0], 16)
            sp.dma_start(raw[1][:, :, :], weights[1]).then_inc(raw_in[1], 16)
            sp.dma_start(wg[:, :, :], w_gate).then_inc(small_in, 16)
            sp.dma_start(bg[:, :], b_gate.broadcast_to([P, EXPERTS])).then_inc(small_in, 16)
            sp.dma_start(tri_sb[:, :, :], tri).then_inc(small_in, 16)

            def phase(g):
                attend, project, goes_out, before = g.flags()
                j = g.half
                if project:
                    if before:
                        need(sp, gl_ready, g.times(2, -2))
                    sp.dma_start(cst[j][:, :], head_consts[g.times(1)]).then_inc(cst_in[j], 16)
                    need(sp, w_lo[j], g.pair(HC, HC))
                    sp.dma_start(raw[j][:, :, :], weights[g.times(1, 2)]).then_inc(raw_in[j], 16)

            for g in range(FIRST):
                phase(Phase(g))
            with loop(mybir.EngineType.SP) as r:
                phase(Phase(FIRST, r))
                phase(Phase(FIRST + 1, r))

            sp.wait_ge(y_done, 8 * (HEADS // 2))
            sp.dma_start(bias[0], b_exp[0].broadcast_to([P, HID])).then_inc(bias_in[0], 16)
            sp.wait_ge(w_lo[1], SPLITS)
            sp.dma_start(raw[1][:, :, 0:HID], experts[1]).then_inc(raw_in[1], 16)
            for e in range(EXPERTS):
                if e + 1 < EXPERTS:
                    need(sp, z_ready, TILES * e)
                    sp.dma_start(bias[(e + 1) % 2], b_exp[e + 1].broadcast_to([P, HID])).then_inc(bias_in[(e + 1) % 2], 16)
                if e + 2 < EXPERTS:
                    sp.wait_ge(w_lo[e % 2], expert_splits(e))
                    sp.dma_start(raw[e % 2][:, :, 0:HID], experts[e + 2]).then_inc(raw_in[e % 2], 16)
            for t in range(TILES):
                sp.wait_ge(f_added, TILES * (EXPERTS - 1) + t + 1)
                sp.dma_start(out[t * P:(t + 1) * P, :], xs[:, t, :]).then_inc(out_sent, 16)
            sp.wait_ge(out_sent, 16 * TILES)

        @block.gpsimd
        def _(pool):
            nc.gpsimd.memset(ident[:, :], 0.0).then_inc(ident_made, 1)
            pool.wait_ge(ident_made, 1)
            nc.gpsimd.affine_select(out=ident[:, :], in_=ident[:, :], compare_op=ALU.not_equal, fill=1.0,
                                    base=0, pattern=[[-1, P]], channel_multiplier=1).then_inc(ident_made, 1)
            nc.gpsimd.memset(ones[:, :], 1.0).then_inc(zeroed, 1)
            nc.gpsimd.memset(sqacc[:, :], 0.0).then_inc(zeroed, 1)
            pool.wait_ge(zeroed, 2)
            pool.wait_ge(xt_done, TILES)
            nc.gpsimd.memset(yacc[:, :, :], 0.0).then_inc(yacc_zeroed, 1)

            def add_squares(g, head, k):
                pool.wait_ge(sq_ready, g.times(2, 2 * head + k + 1))
                need(pool, sq_added, g.times(2, 2 * head + k))
                cols = slice(k * HALF, (k + 1) * HALF)
                nc.gpsimd.tensor_tensor(sqacc[:, cols], sqacc[:, cols], sq[k][:, :], ALU.add).then_inc(sq_added, 1)

            def phase(g):
                attend, project, goes_out, before = g.flags()
                j = g.half
                if before:
                    add_squares(g, -2, 1)
                if project:
                    pool.wait_ge(cst_in[j], g.pair(16, 16))
                    for k in range(2):
                        pool.wait_ge(proj_ready, g.times(BANKS, 2 * k + 1))
                        cols = slice(k * HALF, (k + 1) * HALF)
                        nc.gpsimd.tensor_tensor(
                            qdT[j][:, cols].rearrange("p (c i) -> p c i", i=P),
                            qT[j][:, cols].rearrange("p (c i) -> p c i", i=P),
                            cst[j][:, QD:QD + P].unsqueeze(1).broadcast_to([P, HALF // P, P]),
                            ALU.mult).then_inc(qd_ready, 1)
                if attend:
                    add_squares(g, -1, 0)

            for g in range(FIRST):
                phase(Phase(g))
            with loop(mybir.EngineType.Pool) as r:
                phase(Phase(FIRST, r))
                phase(Phase(FIRST + 1, r))
            for g in (HEADS, HEADS + 1):
                phase(Phase(g))

            for n in range(EXPERTS * TILES):
                t = n % TILES
                pool.wait_ge(relu_ready, n + 1)
                if n >= TILES:
                    pool.wait_ge(f_added, n - TILES + 1)
                else:
                    pool.wait_ge(xn_ready, TILES + t + 1)
                nc.gpsimd.tensor_tensor(xs[:, t, :], xs[:, t, :], relu[n % 2][:, :], ALU.add).then_inc(f_added, 1)

        @block.scalar
        def _(act):
            def roots(m):
                act.wait_ge(var_ready, m + 1)
                if m < GROUPS:
                    cols = slice(m * GROUP, (m + 1) * GROUP)
                elif m == GROUPS:
                    cols = slice(0, TILES)
                else:
                    cols = slice((m - GROUPS - 1) * GROUP, (m - GROUPS) * GROUP)
                nc.scalar.activation(root[:, cols], var[:, cols], ACT.Sqrt).then_inc(root_ready, 1)

            def x_hi(n):
                t = n % TILES
                act.wait_ge(xt_done, n + 1)
                nc.scalar.activation(xh[:, :, t * P:(t + 1) * P],
                                     ps_proj[n % 2][:, :].rearrange("p (c i) -> p c i", i=P),
                                     ACT.Copy).then_inc(xh_ready, 1)

            def w_hi_chunk(j, c, cols=WCOLS):
                nc.scalar.activation(wh[j][:, c, 0:cols], raw[j][:, c, 0:cols], ACT.Copy).then_inc(w_hi[j], 1)

            def phase(g):
                attend, project, goes_out, before = g.flags()
                j = g.half
                prev = 1 - j

                def squares(head, k):
                    act.wait_ge(o_done, g.times(2, 2 * head + k + 1))
                    need(act, sq_added, g.times(2, 2 * head + k - 1))
                    nc.scalar.activation(sq[k][:, :], ps_o[k][:, :], ACT.Square).then_inc(sq_ready, 1)

                def gated_hi(head, k):
                    m = (j + head) % 2
                    act.wait_ge(gt_ready, g.times(2, 2 * head + k + 1))
                    nc.scalar.activation(gh[m][:, k * HALF:(k + 1) * HALF], gt[k][:, :], ACT.Copy,
                                         scale=cst[m][:, NW:NW + 1]).then_inc(gh_ready, 1)

                for s in range(TILES):
                    if attend:
                        if s == 0:
                            act.wait_ge(cst_in[prev], g.pair(16, 16 * j))
                        act.wait_ge(t_done, g.times(TILES, s + 1 - TILES))
                        nc.scalar.activation(kn[:, :], ps_t[:, 0:HD], ACT.Copy,
                                             scale=cst[prev][:, KD:KD + 1]).then_inc(kn_ready, 1)
                    if project and j == 0 and s >= 1:
                        act.wait_ge(v_done, g.pair(TILES, s))
                        nc.scalar.activation(v[:, s - 1, :], ps_vo[:, 0:2 * HD], ACT.Silu).then_inc(v_ready, 1)
                    if before and s == 0:
                        squares(-2, 1)
                    if before and s == 1:
                        if j == 0:
                            need(act, y_done, g.pair(TILES, -TILES))
                        gated_hi(-2, 1)
                    if attend and s == 4:
                        squares(-1, 0)
                    if attend and s == 5:
                        if goes_out:
                            act.wait_ge(y_done, g.pair(TILES, 4 - TILES))
                        gated_hi(-1, 0)
                    if project:
                        for b, (what, th) in enumerate(ORDER):
                            if (HC * b + HC - 1) // PIECES != s:
                                continue
                            act.wait_ge(proj_done, g.times(BANKS, b + 1))
                            if what == "g" and before:
                                act.wait_ge(gt_ready, g.times(2, -2))
                            dst = {"q": qT, "k": kT, "g": gT}[what][j][:, th * HALF:(th + 1) * HALF]
                            src = ps_proj[b % 2][:, :]
                            if what == "g":
                                nc.scalar.activation(dst, src, ACT.Tanh, scale=0.5).then_inc(proj_ready, 1)
                            else:
                                nc.scalar.activation(dst, src, ACT.Silu).then_inc(proj_ready, 1)
                    if s % 2 == 0 and g.times(1) is not None and (g.reg is not None or g.base + 1 < LAST):
                        if s == 0:
                            act.wait_ge(raw_in[prev], g.pair(16, 16 + 16 * j))
                            if j == 1:
                                act.wait_ge(v_done, g.pair(TILES, TILES))
                            elif before:
                                act.wait_ge(proj_done, g.times(BANKS))
                                need(act, y_done, g.pair(TILES, -TILES))
                        w_hi_chunk(prev, s // 2)
                if project and j == 0:
                    act.wait_ge(v_done, g.pair(TILES, TILES))
                    nc.scalar.activation(v[:, TILES - 1, :], ps_vo[:, 0:2 * HD], ACT.Silu).then_inc(v_ready, 1)

            for m in range(GROUPS):
                roots(m)
                for t in range(m * GROUP, (m + 1) * GROUP):
                    x_hi(t)
                if m == 0:
                    act.wait_ge(raw_in[0], 16)
                w_hi_chunk(0, m)
            for g in range(FIRST):
                phase(Phase(g))
            with loop(mybir.EngineType.Activation) as r:
                phase(Phase(FIRST, r))
                phase(Phase(FIRST + 1, r))
            for g in (HEADS, HEADS + 1):
                phase(Phase(g))

            roots(GROUPS)
            act.wait_ge(small_in, 3 * 16)
            nc.scalar.activation(wgh[:, :, :], wg[:, :, :], ACT.Copy).then_inc(wg_hi, 1)
            for m in range(GROUPS):
                roots(GROUPS + 1 + m)
                for t in range(m * GROUP, (m + 1) * GROUP):
                    x_hi(TILES + t)

            for e in range(EXPERTS):
                for t in range(TILES):
                    n = TILES * e + t
                    if e == 0 and t % GROUP == 0:
                        act.wait_ge(routed, t // GROUP + 1)
                    act.wait_ge(z_ready, n + 1)
                    if n >= 2:
                        act.wait_ge(f_added, n - 1)
                    nc.scalar.activation(relu[n % 2][:, :], z[n % 2][:, :], ACT.Relu,
                                         scale=route[:, e, t:t + 1]).then_inc(relu_ready, 1)
                    if t % 2 == 0 and e + 1 < EXPERTS:
                        j = (e + 1) % 2
                        if t == 0:
                            act.wait_ge(raw_in[j], 16 * (LAST // 2 + (e + 1) // 2 + (e + 1) % 2))
                            if e >= 1:
                                act.wait_ge(f_done, TILES * e)
                            else:
                                act.wait_ge(y_done, TILES * HEADS // 2)
                        w_hi_chunk(j, t // 2, HID)

        @block.vector
        def _(dve):
            links = [0]

            def link(ins):
                links[0] += 1
                ins.then_inc(step, 1)
                dve.wait_ge(step, links[0])

            def inverse_root(cols, m):
                dve.wait_ge(root_ready, m + 1)
                link(nc.vector.reciprocal(inv[:, cols], root[:, cols]))
                link(nc.vector.tensor_tensor(tmp[:, cols], inv[:, cols], inv[:, cols], ALU.mult))
                link(nc.vector.tensor_tensor(tmp[:, cols], tmp[:, cols], var[:, cols], ALU.mult))
                link(nc.vector.tensor_scalar(tmp[:, cols], tmp[:, cols], -0.5, 1.5, ALU.mult, ALU.add))
                link(nc.vector.tensor_tensor(rstd[:, cols], inv[:, cols], tmp[:, cols], ALU.mult))

            def norm_stats(m):
                for t in range(m * GROUP, (m + 1) * GROUP):
                    link(nc.vector.bn_stats(stats[:, t, :], xs[:, t, :]))
                    link(nc.vector.bn_aggr(mv[:, t, :], stats[:, t, :]))
                cols = slice(m * GROUP, (m + 1) * GROUP)
                nc.vector.tensor_scalar(var[:, cols], mv[:, cols, 1], EPS, None, ALU.add).then_inc(var_ready, 1)

            def normalise(m, first_root):
                inverse_root(slice(m * GROUP, (m + 1) * GROUP), first_root + m)
                for t in range(m * GROUP, (m + 1) * GROUP):
                    nc.vector.tensor_scalar(yacc[:, t, :], xs[:, t, :], mv[:, t, 0:1], rstd[:, t:t + 1],
                                            ALU.subtract, ALU.mult).then_inc(xn_ready, 1)

            def x_lo(n):
                t = n % TILES
                dve.wait_ge(xh_ready, n + 1)
                cols = slice(t * P, (t + 1) * P)
                nc.vector.tensor_tensor(xl[:, :, cols], ps_proj[n % 2][:, :].rearrange("p (c i) -> p c i", i=P),
                                        xh[:, :, cols].bitcast(F32), ALU.subtract).then_inc(xl_ready, 1)

            def w_lo_chunk(j, c, count, cols=WCOLS):
                dve.wait_ge(w_hi[j], count)
                nc.vector.tensor_tensor(wl[j][:, c, 0:cols], raw[j][:, c, 0:cols],
                                        wh[j][:, c, 0:cols].bitcast(F32), ALU.subtract).then_inc(w_lo[j], 1)

            def phase(g):
                attend, project, goes_out, before = g.flags()
                j = g.half
                prev = 1 - j

                def gated(head, k):
                    m = (j + head) % 2
                    dve.wait_ge(sq_ready, g.times(2, 2 * head + k + 1))
                    dve.wait_ge(proj_ready, g.times(BANKS, BANKS * head + 5 + k))
                    nc.vector.scalar_tensor_tensor(gt[k][:, :], gT[m][:, k * HALF:(k + 1) * HALF], 1.0,
                                                   ps_o[k][:, :], ALU.add, ALU.mult).then_inc(gt_ready, 1)

                def gated_lo(head, k):
                    m = (j + head) % 2
                    cols = slice(k * HALF, (k + 1) * HALF)
                    dve.wait_ge(gh_ready, g.times(2, 2 * head + k + 1))
                    nc.vector.scalar_tensor_tensor(gl[m][:, cols], gt[k][:, :], cst[m][:, NW:NW + 1],
                                                   gh[m][:, cols].bitcast(F32),
                                                   ALU.mult, ALU.subtract).then_inc(gl_ready, 1)

                def add_y(t):
                    dve.wait_ge(y_done, g.pair(TILES, t + 1 - TILES))
                    nc.vector.tensor_tensor(yacc[:, t, :], yacc[:, t, :], ps_vo[:, :], ALU.add).then_inc(y_added, 1)

                for s in range(TILES):
                    if attend:
                        if s == 0:
                            dve.wait_ge(cst_in[prev], g.pair(16, 16 * j))
                        dve.wait_ge(s_done, g.times(TILES, s + 1 - TILES))
                        nc.vector.tensor_tensor(pm[:, :], ps_s[:, 0:P], cst[prev][:, MASK:MASK + P],
                                                ALU.mult).then_inc(pm_ready, 1)
                    if goes_out and s >= 1:
                        add_y(s - 1)
                    if before and s == 0:
                        gated(-2, 1)
                    if attend and s == 4:
                        gated(-1, 0)
                    if before and s == 1:
                        gated_lo(-2, 1)
                    if attend and s == 5:
                        gated_lo(-1, 0)
                    if attend and s < KVN:
                        dve.wait_ge(kv_done, g.times(KVN, s + 1 - KVN))
                        if s == 0:
                            nc.vector.tensor_copy(kv[1][:, :], ps_kv[:, 0:HD]).then_inc(kv_ready, 1)
                        else:
                            dve.wait_ge(kv_ready, g.times(KVN, s - KVN))
                            nc.vector.scalar_tensor_tensor(kv[(s + 1) % 2][:, :], kv[s % 2][:, :],
                                                           cst[prev][:, BD:BD + 1], ps_kv[:, 0:HD],
                                                           ALU.mult, ALU.add).then_inc(kv_ready, 1)
                    if s % 2 == 1 and (g.reg is not None or g.base + 1 < LAST):
                        c = s // 2
                        w_lo_chunk(prev, c, g.pair(HC, c + 1 + HC * j))
                if goes_out:
                    add_y(TILES - 1)

            for m in range(GROUPS):
                for t in range(m * GROUP, (m + 1) * GROUP):
                    dve.wait_ge(x_in[t], 16)
                norm_stats(m)
                if m >= 1:
                    for t in range((m - 1) * GROUP, m * GROUP):
                        x_lo(t)
                    w_lo_chunk(0, m - 1, m)
                normalise(m, 0)
            for t in range(TILES - GROUP, TILES):
                x_lo(t)
            w_lo_chunk(0, HC - 1, HC)
            dve.wait_ge(yacc_zeroed, 1)
            for g in range(FIRST):
                phase(Phase(g))
            with loop(mybir.EngineType.DVE) as r:
                phase(Phase(FIRST, r))
                phase(Phase(FIRST + 1, r))
            for g in (HEADS, HEADS + 1):
                phase(Phase(g))

            dve.wait_ge(rms_done, 1)
            nc.vector.tensor_scalar(var[:, :], ps_t[:, 0:2 * TILES:2], 1.0 / (HEADS * HD), EPS,
                                    ALU.mult, ALU.add).then_inc(var_ready, 1)
            inverse_root(slice(0, TILES), GROUPS)
            link(nc.vector.tensor_scalar(rstd[:, :], rstd[:, :], 0.5, None, ALU.mult))
            for t in range(TILES):
                last = nc.vector.scalar_tensor_tensor(xs[:, t, :], yacc[:, t, :], rstd[:, t:t + 1], xs[:, t, :],
                                                      ALU.mult, ALU.add)
                if t == TILES - 1:
                    link(last)
            dve.wait_ge(wg_hi, 1)
            nc.vector.tensor_tensor(wgl[:, :, :], wg[:, :, :], wgh[:, :, :].bitcast(F32),
                                    ALU.subtract).then_inc(wg_lo, 1)

            def choose(m):
                dve.wait_ge(logit_done, m + 1)
                ps = (ps_s, ps_kv)[m % 2]
                for t in range(m * GROUP, (m + 1) * GROUP):
                    c = EXPERTS * (t - m * GROUP)
                    link(nc.vector.tensor_tensor(lg[:, t, :], ps[:, c:c + EXPERTS], bg[:, :], ALU.add))
                    other = lg[:, t, :].unsqueeze(1).broadcast_to([P, EXPERTS, EXPERTS])
                    own = lg[:, t, :].unsqueeze(2).broadcast_to([P, EXPERTS, EXPERTS])
                    link(nc.vector.tensor_tensor(more[:, :, :], other, own, ALU.is_gt))
                    link(nc.vector.tensor_tensor(same[:, :, :], other, own, ALU.is_equal))
                    link(nc.vector.tensor_tensor(same[:, :, :], same[:, :, :], tri_sb[:, :, :], ALU.mult))
                    link(nc.vector.tensor_tensor(more[:, :, :], more[:, :, :], same[:, :, :], ALU.add))
                    link(nc.vector.tensor_reduce(rank[:, t, :], more[:, :, :], AX_X, ALU.add))
                    last = nc.vector.tensor_scalar(route[:, :, t], rank[:, t, :], TOP_K - 0.5, 1.0 / TOP_K,
                                                   ALU.is_lt, ALU.mult)
                last.then_inc(routed, 1)

            for m in range(GROUPS):
                norm_stats(m)
                if m >= 1:
                    for t in range((m - 1) * GROUP, m * GROUP):
                        x_lo(TILES + t)
                normalise(m, GROUPS + 1)
            for t in range(TILES - GROUP, TILES):
                x_lo(TILES + t)
            for m in range(GROUPS):
                choose(m)

            for e in range(EXPERTS):
                dve.wait_ge(bias_in[e % 2], 16 * (e // 2 + 1))
                for t in range(TILES):
                    n = TILES * e + t
                    dve.wait_ge(f_done, n + 1)
                    if n >= 2:
                        dve.wait_ge(relu_ready, n - 1)
                    nc.vector.tensor_tensor(z[n % 2][:, :], ps_ffn[n % 4][:, :], bias[e % 2],
                                            ALU.add).then_inc(z_ready, 1)
                    if t % 2 == 1 and e + 1 < EXPERTS:
                        w_lo_chunk((e + 1) % 2, t // 2, expert_splits(e + 1) - HC + t // 2 + 1, HID)

        @block.tensor
        def _(pe):
            def three(ps, stat, mov, first, last):
                nc.tensor.matmul(ps, stat[0], mov[1], start=first, stop=False)
                nc.tensor.matmul(ps, stat[0], mov[0], start=False, stop=False)
                return nc.tensor.matmul(ps, stat[1], mov[0], start=False, stop=last)

            def transpose_x(n):
                t = n % TILES
                pe.wait_ge(xn_ready, n + 1)
                if n >= 2:
                    pe.wait_ge(xl_ready, n - 1)
                for c in range(HC):
                    last = nc.tensor.transpose(ps_proj[n % 2][:, c * P:(c + 1) * P],
                                               yacc[:, t, c * P:(c + 1) * P], ident[:, :])
                last.then_inc(xt_done, 1)

            def phase(g):
                attend, project, goes_out, before = g.flags()
                j = g.half
                prev = 1 - j
                for s in range(TILES):
                    tile = slice(s * P, (s + 1) * P)
                    if attend:
                        if s % 4 == 0:
                            pe.wait_ge(proj_ready, g.times(BANKS, s // 2 + 2 - BANKS))
                        need(pe, kn_ready, g.times(TILES, s - TILES))
                        nc.tensor.transpose(ps_t[:, 0:HD], kT[prev][:, tile], ident[:, :]).then_inc(t_done, 1)
                        need(pe, pm_ready, g.times(TILES, s - TILES))
                        nc.tensor.matmul(ps_s[:, 0:P], kT[prev][:, tile], qT[prev][:, tile],
                                         start=True, stop=True).then_inc(s_done, 1)
                    if project:
                        for n in range(PIECES * s, PIECES * (s + 1)):
                            b, c = n // HC, n % HC
                            what, th = ORDER[b]
                            if g.reg is None and g.base == 0 and n == 0:
                                pe.wait_ge(xl_ready, TILES)
                            if b == 0:
                                pe.wait_ge(w_lo[j], g.pair(HC, c + 1))
                            if c == 0:
                                need(pe, proj_ready, g.times(BANKS, b - 1))
                            w = slice(COL[what], COL[what] + HD)
                            x0 = slice(th * HALF, (th + 1) * HALF)
                            last = three(ps_proj[b % 2][:, :], (wh[j][:, c, w], wl[j][:, c, w]),
                                         (xh[:, c, x0], xl[:, c, x0]), c == 0, c == HC - 1)
                            if c == HC - 1:
                                last.then_inc(proj_done, 1)
                    if attend:
                        vs = v[:, s, prev * HD:(prev + 1) * HD]
                        if s < KVN:
                            pe.wait_ge(kn_ready, g.times(TILES, s + 1 - TILES))
                            need(pe, kv_ready, g.times(KVN, s - KVN))
                            if s == 1 and j == 1:
                                pe.wait_ge(v_ready, g.pair(TILES, TILES))
                            nc.tensor.matmul(ps_kv[:, 0:HD], kn[:, :], vs, start=True, stop=True).then_inc(kv_done, 1)
                        o = ps_o[s // 4][:, (s % 4) * P:(s % 4 + 1) * P]
                        if s % 4 == 0:
                            need(pe, gt_ready, g.times(2, s // 4 - 3))
                        pe.wait_ge(pm_ready, g.times(TILES, s + 1 - TILES))
                        last = nc.tensor.matmul(o, vs, pm[:, :], start=True, stop=s == 0)
                        if s:
                            pe.wait_ge(kv_ready, g.times(KVN, s - KVN))
                            if s in (1, 4):
                                pe.wait_ge(qd_ready, g.times(2, s // 4 - 1))
                            last = nc.tensor.matmul(o, kv[s % 2][:, :], qdT[prev][:, tile], start=False, stop=True)
                        if s % 4 == 3:
                            last.then_inc(o_done, 1)
                    if project and j == 0:
                        if s == 0:
                            pe.wait_ge(w_lo[0], g.pair(HC, HC))
                            need(pe, y_added, g.pair(TILES, -TILES))
                        else:
                            pe.wait_ge(v_ready, g.pair(TILES, s))
                        for c in range(HC):
                            w = slice(V0, V0 + 2 * HD)
                            last = three(ps_vo[:, 0:2 * HD], (xh[:, c, tile], xl[:, c, tile]),
                                         (wh[0][:, c, w], wl[0][:, c, w]), c == 0, c == HC - 1)
                        last.then_inc(v_done, 1)
                    if goes_out:
                        if s == 0:
                            pe.wait_ge(w_lo[1], g.pair(HC, HC))
                            if project:
                                pe.wait_ge(v_ready, g.pair(TILES, TILES))
                        else:
                            pe.wait_ge(y_added, g.pair(TILES, s - TILES))
                        if s % 4 == 0:
                            pe.wait_ge(gl_ready, g.times(2, s // 4 - 3))
                        for m in range(2):
                            w = slice(V0, V0 + 2 * HD)
                            last = three(ps_vo[:, :].rearrange("p (a b) -> p a b", a=2),
                                         (gh[m][:, tile], gl[m][:, tile]),
                                         (wh[1][:, 2 * m:2 * m + 2, w], wl[1][:, 2 * m:2 * m + 2, w]),
                                         m == 0, m == 1)
                        last.then_inc(y_done, 1)

            pe.wait_ge(ident_made, 2)
            for t in range(TILES):
                transpose_x(t)
            for g in range(FIRST):
                phase(Phase(g))
            with loop(mybir.EngineType.PE) as r:
                phase(Phase(FIRST, r))
                phase(Phase(FIRST + 1, r))
            phase(Phase(HEADS))
            phase(Phase(HEADS + 1))

            pe.wait_ge(sq_added, 2 * HEADS)
            pe.wait_ge(zeroed, 2)
            pe.wait_ge(kn_ready, HEADS * TILES)
            for t in range(TILES):
                last = nc.tensor.matmul(ps_t[:, 2 * t:2 * t + 2], sqacc[:, t * P:(t + 1) * P], ones[:, :],
                                        start=True, stop=True)
            last.then_inc(rms_done, 1)

            def expert_tile(e, t):
                n = TILES * e + t
                if t == 0:
                    pe.wait_ge(w_lo[e % 2], expert_splits(e))
                if n >= 4:
                    pe.wait_ge(z_ready, n - 3)
                for c in range(HC):
                    tile = slice(t * P, (t + 1) * P)
                    last = three(ps_ffn[n % 4][:, :], (xh[:, c, tile], xl[:, c, tile]),
                                 (wh[e % 2][:, c, 0:HID], wl[e % 2][:, c, 0:HID]), c == 0, c == HC - 1)
                last.then_inc(f_done, 1)

            for m in range(GROUPS):
                for t in range(m * GROUP, (m + 1) * GROUP):
                    transpose_x(TILES + t)
            pe.wait_ge(wg_lo, 1)
            for m in range(GROUPS):
                pe.wait_ge(xl_ready, TILES + (m + 1) * GROUP)
                if m >= 2:
                    pe.wait_ge(routed, m - 1)
                for t in range(m * GROUP, (m + 1) * GROUP):
                    ps = (ps_s, ps_kv)[m % 2]
                    o = EXPERTS * (t - m * GROUP)
                    for c in range(HC):
                        tile = slice(t * P, (t + 1) * P)
                        last = three(ps[:, o:o + EXPERTS], (xh[:, c, tile], xl[:, c, tile]),
                                     (wgh[:, c, :], wgl[:, c, :]), c == 0, c == HC - 1)
                last.then_inc(logit_done, 1)
            for e in range(EXPERTS):
                for t in range(TILES):
                    expert_tile(e, t)


def head_constants():
    layer_idx, n_layers = 1, 32
    base = 1.0 / 2.0 ** (8.0 / HEADS)
    factor = 1.0 - layer_idx / (n_layers - 1 + 1e-05) + 1e-05
    slope = (base ** (np.arange(HEADS) + 1.0) * factor)[:, None, None]
    r = np.arange(P) + 1.0
    diff = r[None, :] - r[:, None]
    mask = np.where(diff >= 0, np.exp(-slope * np.maximum(diff, 0)), 0.0)
    qd = np.broadcast_to(np.exp(-slope * r), (HEADS, P, P))
    kd = np.exp(-slope * (P - r)[:, None])
    bd = np.broadcast_to(np.exp(-slope * P), (HEADS, P, 1))
    return np.concatenate([mask, qd, kd, bd], axis=2).astype(np.float32)


def kernel(**inputs):
    import concourse.bacc as bacc
    from concourse.bass_utils import run_bass_kernel_spmd

    a = {k.split("_", 1)[1]: np.asarray(val) for k, val in inputs.items()}
    x = np.ascontiguousarray(a["attn_hidden_states"]).reshape(TOKENS, HID)

    def transposed(w):
        return w.T.reshape(HC, P, -1).transpose(1, 0, 2)

    qkv = a["attn_qkv_w"].reshape(HEADS, 3, HD, HID)
    gate = a["attn_gate_w"].reshape(HEADS, HD, HID)
    out_w = a["attn_out_w"]
    weights = np.zeros((LAST, P, HC, WCOLS), np.float32)
    for g in range(LAST):
        if g < HEADS:
            weights[g, :, :, 0:HD] = transposed(qkv[g, 0])
            weights[g, :, :, HD:2 * HD] = transposed(qkv[g, 1])
            weights[g, :, :, 2 * HD:3 * HD] = transposed(gate[g])
            if g % 2 == 0:
                weights[g, :, :, V0:V0 + HD] = transposed(qkv[g, 2])
                weights[g, :, :, V0 + HD:V0 + 2 * HD] = transposed(qkv[g + 1, 2])
        if g % 2 == 1 and g >= 3:
            for m in range(2):
                h = g - 3 + m
                w = out_w[:, h * HD:(h + 1) * HD].T
                weights[g, :, 2 * m:2 * m + 2, V0:V0 + 2 * HD] = w.reshape(HD, 2, 2 * HD)
    experts = a["ffn_W_e"].reshape(EXPERTS, HC, P, HID).transpose(0, 2, 1, 3)
    weights[HEADS, :, :, 0:HID] = experts[0]
    norm_w = a["attn_norm_w"].reshape(HEADS, HD, 1)
    consts = np.concatenate([head_constants(), norm_w], axis=2)
    tri = np.broadcast_to(np.tril(np.ones((EXPERTS, EXPERTS), np.float32), -1), (P, EXPERTS, EXPERTS))

    arrays = {
        "x": x, "weights": weights, "experts": experts, "head_consts": consts,
        "w_gate": a["ffn_W_gate"].reshape(HC, P, EXPERTS).transpose(1, 0, 2),
        "b_gate": a["ffn_b_gate"].reshape(1, EXPERTS), "b_exp": a["ffn_b_e"].reshape(EXPERTS, 1, HID),
        "tri": tri,
    }
    arrays = {k: np.ascontiguousarray(val) for k, val in arrays.items()}
    nc = bacc.Bacc("TRN2", target_bir_lowering=False, num_devices=1)
    aps = [nc.dram_tensor(k, val.shape, F32, kind="ExternalInput").ap() for k, val in arrays.items()]
    out = nc.dram_tensor("out", (TOKENS, HID), F32, kind="ExternalOutput").ap()
    layer(nc, *aps, out)
    r = run_bass_kernel_spmd(nc, [arrays], core_ids=[0])
    return r.results[0]["out"].reshape(1, TOKENS, HID)
```

```python
from contextlib import ExitStack

import numpy as np

import concourse.bass as bass
from concourse import mybir
from concourse.alu_op_type import AluOpType as ALU

F32 = mybir.dt.float32
F32R = mybir.dt.float32r
ACT = mybir.ActivationFunctionType
AX_X = mybir.AxisListType.X

P = 128
TOKENS, HID = 1024, 512
HEADS, HD = 32, 128
EXPERTS, TOP_K = 8, 2
EPS = 1e-5
TILES = TOKENS // P
HC = HID // P
HALF = TOKENS // 2
WCOLS = 3 * HD + 2 * HD
V0 = 3 * HD
BANKS = 6
ORDER = [("q", 0), ("k", 0), ("q", 1), ("k", 1), ("g", 0), ("g", 1)]
COL = {"q": 0, "k": HD, "g": 2 * HD}
PIECES = BANKS * HC // TILES
MASK, QD, KD, BD, NW = 0, HD, 2 * HD, 2 * HD + 1, 2 * HD + 2
CCOLS = 2 * HD + 3
KVN = TILES - 1
LAST = HEADS + 2
FIRST = 4


class Phase:

    def __init__(self, base, reg=None):
        self.base, self.reg, self.half = base, reg, base % 2

    def times(self, n, plus=0):
        c = n * self.base + plus
        return c if self.reg is None else self.reg * (2 * n) + c

    def pair(self, n, plus=0):
        c = n * (self.base // 2) + plus
        return c if self.reg is None else self.reg * n + c

    def flags(self):
        if self.reg is not None:
            return True, True, self.half == 1, True
        g = self.base
        return 1 <= g <= HEADS, g < HEADS, self.half == 1 and 3 <= g < HEADS, g >= 2


def need(eng, semaphore, value):
    if not isinstance(value, int) or value > 0:
        eng.wait_ge(semaphore, value)


def layer(nc, x, weights, experts, head_consts, w_gate, b_gate, b_exp, tri, out):
    with ExitStack() as ctx:
        def sb(name, shape, dt=F32):
            return ctx.enter_context(nc.sbuf_tensor(name, shape, dt))

        def psum(name):
            return ctx.enter_context(nc.psum_tensor(name, [P, 512], F32))

        def sem(name):
            return ctx.enter_context(nc.semaphore(name))

        xs = sb("xs", [P, TILES, HID])
        yacc = sb("yacc", [P, TILES, HID])
        xh = sb("xh", [P, HC, TOKENS], F32R)
        xl = sb("xl", [P, HC, TOKENS], F32R)
        raw = [sb(f"raw{j}", [P, HC, WCOLS]) for j in range(2)]
        wh = [sb(f"wh{j}", [P, HC, WCOLS], F32R) for j in range(2)]
        wl = [sb(f"wl{j}", [P, HC, WCOLS], F32R) for j in range(2)]
        qT = [sb(f"qT{j}", [P, TOKENS]) for j in range(2)]
        kT = [sb(f"kT{j}", [P, TOKENS]) for j in range(2)]
        gT = [sb(f"gT{j}", [P, TOKENS]) for j in range(2)]
        qdT = [sb(f"qdT{j}", [P, TOKENS]) for j in range(2)]
        v = sb("v", [P, TILES, 2 * HD])
        cst = [sb(f"cst{j}", [P, CCOLS]) for j in range(2)]
        kn_sb = sb("kn", [P, HD])
        pm_sb = sb("pm", [P, P])
        kv = [sb(f"kv{j}", [P, HD]) for j in range(2)]
        sq = [sb(f"sq{j}", [P, HALF]) for j in range(2)]
        gt = [sb(f"gt{j}", [P, HALF]) for j in range(2)]
        gh = [sb(f"gh{j}", [P, TOKENS], F32R) for j in range(2)]
        gl = [sb(f"gl{j}", [P, TOKENS], F32R) for j in range(2)]
        sqacc = sb("sqacc", [P, TOKENS])
        ident = sb("ident", [P, P])
        ones = sb("ones", [P, 2])
        stats = sb("stats", [P, TILES, 6])
        mv = sb("mv", [P, TILES, 2])
        var = sb("var", [P, TILES])
        root = sb("root", [P, TILES])
        inv = sb("inv", [P, TILES])
        tmp = sb("tmp", [P, TILES])
        rstd = sb("rstd", [P, TILES])
        rs = sb("rs", [P, TILES])
        negm = sb("negm", [P, TILES])
        wgh = sb("wgh", [P, HC, P], F32R)
        wgl = sb("wgl", [P, HC, P], F32R)
        bg = sb("bg", [EXPERTS, 1])
        tri_sb = sb("tri_sb", [P, EXPERTS, EXPERTS])
        lg = sb("lg", [P, TILES // 2, EXPERTS])
        more = sb("more", [P, TILES // 2, EXPERTS, EXPERTS])
        same = sb("same", [P, TILES // 2, EXPERTS, EXPERTS])
        rank = sb("rank", [P, TILES, EXPERTS])
        route = sb("route", [P, EXPERTS, TILES])
        bias = [v[:, 2 * j:2 * j + 2, :].rearrange("p a b -> p (a b)") for j in range(2)]
        z, relu = gt, sq
        wg = qT[0][:, 0:HC * P].rearrange("p (c n) -> p c n", c=HC)
        lgT = qT[1][0:EXPERTS, :]

        ps_proj = [psum(f"ps_proj{j}") for j in range(2)]
        ps_vo = psum("ps_vo")
        ps_t = psum("ps_t")
        ps_s = psum("ps_s")
        ps_kv = psum("ps_kv")
        ps_o = [psum(f"ps_o{j}") for j in range(2)]
        ps_out = [ps_vo, ps_proj[0], ps_proj[1], ps_kv]

        x_in = [sem(f"x_in{t}") for t in range(TILES)]
        raw_in = [sem(f"raw_in{j}") for j in range(2)]
        cst_in = [sem(f"cst_in{j}") for j in range(2)]
        small_in = sem("small_in")
        bias_in = [sem(f"bias_in{j}") for j in range(2)]
        out_sent = sem("out_sent")
        ident_made = sem("ident_made")
        zeroed = sem("zeroed")
        yacc_zeroed = sem("yacc_zeroed")
        var_ready = sem("var_ready")
        root_ready = sem("root_ready")
        xn_ready = sem("xn_ready")
        xt_done = sem("xt_done")
        xh_ready = sem("xh_ready")
        xl_ready = sem("xl_ready")
        w_hi = [sem(f"w_hi{j}") for j in range(2)]
        w_lo = [sem(f"w_lo{j}") for j in range(2)]
        wg_hi = sem("wg_hi")
        wg_lo = sem("wg_lo")
        proj_done = sem("proj_done")
        proj_ready = sem("proj_ready")
        qd_ready = sem("qd_ready")
        v_done = sem("v_done")
        v_ready = sem("v_ready")
        t_done = sem("t_done")
        kn_ready = sem("kn_ready")
        s_done = sem("s_done")
        pm_ready = sem("pm_ready")
        kv_done = sem("kv_done")
        kv_ready = sem("kv_ready")
        o_done = sem("o_done")
        sq_ready = sem("sq_ready")
        sq_added = sem("sq_added")
        gt_ready = sem("gt_ready")
        gh_ready = sem("gh_ready")
        gl_ready = sem("gl_ready")
        y_done = sem("y_done")
        y_added = sem("y_added")
        y_scaled = sem("y_scaled")
        y_based = sem("y_based")
        x2_ready = sem("x2_ready")
        norm_ready = sem("norm_ready")
        rs_ready = sem("rs_ready")
        logit_ready = sem("logit_ready")
        logit_turned = sem("logit_turned")
        rms_done = sem("rms_done")
        logit_done = sem("logit_done")
        routed = sem("routed")
        f_done = sem("f_done")
        z_ready = sem("z_ready")
        relu_ready = sem("relu_ready")
        f_added = sem("f_added")
        step = sem("step")

        block = ctx.enter_context(nc.Block())
        G1 = TILES // 2
        G2 = 2
        GROUPS = TILES // G2
        SCALED = 3
        SPLITS = HC * (LAST // 2)

        def expert_splits(e):
            return SPLITS + HC * (e // 2 + e % 2)

        def chunk_buffers(project):
            own = (ps_t, ps_s, kn_sb, pm_sb)
            return [own] if project else [own, (ps_proj[0], ps_proj[1], kT[0][:, 0:HD], kT[0][:, HD:HD + P])]

        def loop(engine):
            return nc.Fori(0, (HEADS - FIRST) // 2, engines=[engine], hint_back_edge=True)

        @block.sync
        def _(sp):
            for t in range(G1):
                sp.dma_start(xs[:, t, :], x[t * P:(t + 1) * P, :]).then_inc(x_in[t], 16)
            sp.dma_start(raw[0][:, :, :], weights[0]).then_inc(raw_in[0], 16)
            for t in range(G1, TILES):
                sp.dma_start(xs[:, t, :], x[t * P:(t + 1) * P, :]).then_inc(x_in[t], 16)
            sp.dma_start(raw[1][:, :, :], weights[1]).then_inc(raw_in[1], 16)
            sp.dma_start(bg[:, :], b_gate).then_inc(small_in, 16)
            sp.dma_start(tri_sb[:, :, :], tri).then_inc(small_in, 16)

            def phase(g):
                attend, project, goes_out, before = g.flags()
                j = g.half
                if project:
                    if before:
                        need(sp, gl_ready, g.times(2, -2))
                    sp.dma_start(cst[j][:, :], head_consts[g.times(1)]).then_inc(cst_in[j], 16)
                    need(sp, w_lo[j], g.pair(HC, HC))
                    sp.dma_start(raw[j][:, :, :], weights[g.times(1, 2)]).then_inc(raw_in[j], 16)

            for g in range(FIRST):
                phase(Phase(g))
            with loop(mybir.EngineType.SP) as r:
                phase(Phase(FIRST, r))
                phase(Phase(FIRST + 1, r))

            sp.wait_ge(o_done, 2 * (HEADS - 1))
            sp.dma_start(wg, w_gate).then_inc(small_in, 16)
            sp.wait_ge(o_done, 2 * HEADS)
            sp.dma_start(bias[0], b_exp[0].broadcast_to([P, HID])).then_inc(bias_in[0], 16)
            sp.wait_ge(w_lo[1], SPLITS)
            sp.dma_start(raw[1][:, :, 0:HID], experts[1]).then_inc(raw_in[1], 16)
            for e in range(EXPERTS):
                if e + 1 < EXPERTS:
                    need(sp, z_ready, TILES * e)
                    sp.dma_start(bias[(e + 1) % 2], b_exp[e + 1].broadcast_to([P, HID])).then_inc(bias_in[(e + 1) % 2], 16)
                if e + 2 < EXPERTS:
                    sp.wait_ge(w_lo[e % 2], expert_splits(e))
                    sp.dma_start(raw[e % 2][:, :, 0:HID], experts[e + 2]).then_inc(raw_in[e % 2], 16)
            for t in range(TILES):
                sp.wait_ge(f_added, TILES * (EXPERTS - 1) + t + 1)
                sp.dma_start(out[t * P:(t + 1) * P, :], xs[:, t, :]).then_inc(out_sent, 16)
            sp.wait_ge(out_sent, 16 * TILES)

        @block.gpsimd
        def _(pool):
            nc.gpsimd.memset(ident[:, :], 0.0).then_inc(ident_made, 1)
            pool.wait_ge(ident_made, 1)
            nc.gpsimd.affine_select(out=ident[:, :], in_=ident[:, :], compare_op=ALU.not_equal, fill=1.0,
                                    base=0, pattern=[[-1, P]], channel_multiplier=1).then_inc(ident_made, 1)
            nc.gpsimd.memset(ones[:, :], 1.0).then_inc(zeroed, 1)
            nc.gpsimd.memset(sqacc[:, :], 0.0).then_inc(zeroed, 1)
            for c in range(HC):
                pool.wait_ge(w_hi[0], c + 1)
                nc.gpsimd.tensor_tensor(wl[0][:, c, :], raw[0][:, c, :], wh[0][:, c, :].bitcast(F32),
                                        ALU.subtract).then_inc(w_lo[0], 1)
            pool.wait_ge(zeroed, 2)
            pool.wait_ge(xt_done, TILES)
            nc.gpsimd.memset(yacc[:, :, :], 0.0).then_inc(yacc_zeroed, 1)

            def add_squares(g, head, k):
                pool.wait_ge(sq_ready, g.times(2, 2 * head + k + 1))
                need(pool, sq_added, g.times(2, 2 * head + k))
                cols = slice(k * HALF, (k + 1) * HALF)
                nc.gpsimd.tensor_tensor(sqacc[:, cols], sqacc[:, cols], sq[k][:, :], ALU.add).then_inc(sq_added, 1)

            def phase(g):
                attend, project, goes_out, before = g.flags()
                j = g.half
                if before:
                    add_squares(g, -2, 1)
                if project:
                    pool.wait_ge(cst_in[j], g.pair(16, 16))
                    for k in range(2):
                        pool.wait_ge(proj_ready, g.times(BANKS, 2 * k + 1))
                        cols = slice(k * HALF, (k + 1) * HALF)
                        nc.gpsimd.tensor_tensor(
                            qdT[j][:, cols].rearrange("p (c i) -> p c i", i=P),
                            qT[j][:, cols].rearrange("p (c i) -> p c i", i=P),
                            cst[j][:, QD:QD + P].unsqueeze(1).broadcast_to([P, HALF // P, P]),
                            ALU.mult).then_inc(qd_ready, 1)
                if attend:
                    add_squares(g, -1, 0)

            for g in range(FIRST):
                phase(Phase(g))
            with loop(mybir.EngineType.Pool) as r:
                phase(Phase(FIRST, r))
                phase(Phase(FIRST + 1, r))
            for g in (HEADS, HEADS + 1):
                phase(Phase(g))

            for t in range(TILES):
                if t < SCALED:
                    pool.wait_ge(y_scaled, t + 1)
                else:
                    pool.wait_ge(rs_ready, 1)
                    nc.gpsimd.tensor_scalar(yacc[:, t, :], yacc[:, t, :], rs[:, t:t + 1], None,
                                            ALU.mult).then_inc(y_scaled, 1)
                    pool.wait_ge(y_scaled, t + 1)
                nc.gpsimd.tensor_tensor(xs[:, t, :], xs[:, t, :], yacc[:, t, :], ALU.add).then_inc(y_based, 1)

            for n in range(EXPERTS * TILES):
                t = n % TILES
                pool.wait_ge(relu_ready, n + 1)
                if n >= TILES:
                    pool.wait_ge(f_added, n - TILES + 1)
                else:
                    pool.wait_ge(xn_ready, TILES + t + 1)
                nc.gpsimd.tensor_tensor(xs[:, t, :], xs[:, t, :], relu[n % 2][:, :], ALU.add).then_inc(f_added, 1)

        @block.scalar
        def _(act):
            def roots(cols, count):
                act.wait_ge(var_ready, count)
                nc.scalar.activation(root[:, cols], var[:, cols], ACT.Sqrt).then_inc(root_ready, 1)

            def x_hi(n):
                t = n % TILES
                act.wait_ge(xt_done, n + 1)
                nc.scalar.activation(xh[:, :, t * P:(t + 1) * P],
                                     ps_o[n % 2][:, :].rearrange("p (c i) -> p c i", i=P),
                                     ACT.Copy).then_inc(xh_ready, 1)

            def w_hi_chunk(j, c, cols=WCOLS):
                nc.scalar.activation(wh[j][:, c, 0:cols], raw[j][:, c, 0:cols], ACT.Copy).then_inc(w_hi[j], 1)

            def phase(g):
                attend, project, goes_out, before = g.flags()
                j = g.half
                prev = 1 - j

                def squares(head, k):
                    act.wait_ge(o_done, g.times(2, 2 * head + k + 1))
                    need(act, sq_added, g.times(2, 2 * head + k - 1))
                    nc.scalar.activation(sq[k][:, :], ps_o[k][:, :], ACT.Square).then_inc(sq_ready, 1)

                def gated_hi(head, k):
                    m = (j + head) % 2
                    act.wait_ge(gt_ready, g.times(2, 2 * head + k + 1))
                    nc.scalar.activation(gh[m][:, k * HALF:(k + 1) * HALF], gt[k][:, :], ACT.Copy,
                                         scale=cst[m][:, NW:NW + 1]).then_inc(gh_ready, 1)

                for s in range(TILES):
                    if attend:
                        if s == 0:
                            act.wait_ge(cst_in[prev], g.pair(16, 16 * j))
                        act.wait_ge(t_done, g.times(TILES, s + 1 - TILES))
                        turns = chunk_buffers(project)
                        pst, _, kn, _ = turns[s % len(turns)]
                        nc.scalar.activation(kn[:, :], pst[:, 0:HD], ACT.Copy,
                                             scale=cst[prev][:, KD:KD + 1]).then_inc(kn_ready, 1)
                    if project and j == 0 and s >= 1:
                        act.wait_ge(v_done, g.pair(TILES, s))
                        nc.scalar.activation(v[:, s - 1, :], ps_vo[:, 0:2 * HD], ACT.Silu).then_inc(v_ready, 1)
                    if g.reg is None and g.base == 0 and s == 2:
                        for t in range(G1, TILES):
                            x_hi(t)
                    if before and s == 0:
                        squares(-2, 1)
                    if before and s == 1:
                        if j == 0:
                            need(act, y_done, g.pair(TILES, -TILES))
                        gated_hi(-2, 1)
                    if attend and s == 4:
                        squares(-1, 0)
                    if attend and s == 5:
                        if goes_out:
                            act.wait_ge(y_done, g.pair(TILES, 4 - TILES))
                        gated_hi(-1, 0)
                    if project:
                        for b, (what, th) in enumerate(ORDER):
                            if (HC * b + HC - 1) // PIECES != s:
                                continue
                            act.wait_ge(proj_done, g.times(BANKS, b + 1))
                            if what == "g" and before:
                                act.wait_ge(gt_ready, g.times(2, -2))
                            dst = {"q": qT, "k": kT, "g": gT}[what][j][:, th * HALF:(th + 1) * HALF]
                            src = ps_proj[b % 2][:, :]
                            if what == "g":
                                nc.scalar.activation(dst, src, ACT.Tanh, scale=0.5).then_inc(proj_ready, 1)
                            else:
                                nc.scalar.activation(dst, src, ACT.Silu).then_inc(proj_ready, 1)
                    if s % 2 == 0 and (g.reg is not None or g.base + 1 < LAST):
                        if s == 0:
                            act.wait_ge(raw_in[prev], g.pair(16, 16 + 16 * j))
                            if j == 1:
                                act.wait_ge(v_done, g.pair(TILES, TILES))
                            elif before:
                                act.wait_ge(proj_done, g.times(BANKS))
                                need(act, y_done, g.pair(TILES, -TILES))
                        w_hi_chunk(prev, s // 2)
                if project and j == 0:
                    act.wait_ge(v_done, g.pair(TILES, TILES))
                    nc.scalar.activation(v[:, TILES - 1, :], ps_vo[:, 0:2 * HD], ACT.Silu).then_inc(v_ready, 1)

            roots(slice(0, G1), 1)
            act.wait_ge(raw_in[0], 16)
            for c in range(HC):
                x_hi(c)
                if c != 1:
                    w_hi_chunk(0, max(c - 1, 0))
            w_hi_chunk(0, HC - 1)
            roots(slice(G1, TILES), 2)
            for g in range(FIRST):
                phase(Phase(g))
            with loop(mybir.EngineType.Activation) as r:
                phase(Phase(FIRST, r))
                phase(Phase(FIRST + 1, r))
            for g in (HEADS, HEADS + 1):
                phase(Phase(g))

            roots(slice(0, TILES), 3)
            act.wait_ge(small_in, 3 * 16)
            nc.scalar.activation(wgh[:, :, :], wg, ACT.Copy).then_inc(wg_hi, 1)
            act.wait_ge(rs_ready, 1)

            def scale_y(t):
                nc.scalar.activation(yacc[:, t, :], yacc[:, t, :], ACT.Copy,
                                     scale=rs[:, t:t + 1]).then_inc(y_scaled, 1)

            def x2_norm(m):
                roots(slice(m * G2, (m + 1) * G2), 4 + m)
                act.wait_ge(norm_ready, m + 1)
                for t in range(m * G2, (m + 1) * G2):
                    nc.scalar.activation(yacc[:, t, :], xs[:, t, :], ACT.Identity, bias=negm[:, t:t + 1],
                                         scale=rstd[:, t:t + 1]).then_inc(xn_ready, 1)

            def logits(k):
                act.wait_ge(logit_done, k + 1)
                nc.scalar.activation(lgT[:, k * HALF:(k + 1) * HALF], ps_s[0:EXPERTS, :], ACT.Identity,
                                     bias=bg[:, :]).then_inc(logit_ready, 1)

            def weigh(e, t):
                n = TILES * e + t
                if e == 0 and t % (TILES // 2) == 0:
                    act.wait_ge(routed, 2 * t // TILES + 1)
                act.wait_ge(z_ready, n + 1)
                if n >= 2:
                    act.wait_ge(f_added, n - 1)
                nc.scalar.activation(relu[n % 2][:, :], z[n % 2][:, :], ACT.Relu,
                                     scale=route[:, e, t:t + 1]).then_inc(relu_ready, 1)

            def w_hi_expert(e, c):
                j = e % 2
                if c == 0:
                    act.wait_ge(raw_in[j], 16 * (LAST // 2 + e // 2 + e % 2))
                    if e >= 2:
                        act.wait_ge(f_done, TILES * (e - 1))
                    else:
                        act.wait_ge(y_done, TILES * HEADS // 2)
                w_hi_chunk(j, c, HID)

            for t in range(SCALED):
                scale_y(t)
            for m in range(GROUPS):
                x2_norm(m)
                for t in range(m * G2, (m + 1) * G2):
                    x_hi(TILES + t)
            logits(0)
            for t in range(TILES):
                if t in (1, 2, 3, 5):
                    w_hi_expert(1, {1: 0, 2: 1, 3: 2, 5: 3}[t])
                if t == TILES // 2:
                    logits(1)
                weigh(0, t)

            for e in range(1, EXPERTS):
                for t in range(TILES):
                    if t % 2 == 0 and e + 1 < EXPERTS:
                        w_hi_expert(e + 1, t // 2)
                    weigh(e, t)

        @block.vector
        def _(dve):
            links = [0]

            def link(ins):
                links[0] += 1
                ins.then_inc(step, 1)
                dve.wait_ge(step, links[0])

            def inverse_root(cols, count, dst):
                dve.wait_ge(root_ready, count)
                link(nc.vector.reciprocal(inv[:, cols], root[:, cols]))
                link(nc.vector.tensor_tensor(tmp[:, cols], inv[:, cols], inv[:, cols], ALU.mult))
                link(nc.vector.tensor_tensor(tmp[:, cols], tmp[:, cols], var[:, cols], ALU.mult))
                link(nc.vector.tensor_scalar(tmp[:, cols], tmp[:, cols], -0.5, 1.5, ALU.mult, ALU.add))
                link(nc.vector.tensor_tensor(dst[:, cols], inv[:, cols], tmp[:, cols], ALU.mult))

            def norm_stats(t):
                link(nc.vector.bn_stats(stats[:, t, :], xs[:, t, :]))
                link(nc.vector.bn_aggr(mv[:, t, :], stats[:, t, :]))

            def variances(cols):
                nc.vector.tensor_scalar(var[:, cols], mv[:, cols, 1], EPS, None, ALU.add).then_inc(var_ready, 1)

            def normalise(cols, count):
                inverse_root(cols, count, rstd)
                for t in range(cols.start, cols.stop):
                    nc.vector.tensor_scalar(yacc[:, t, :], xs[:, t, :], mv[:, t, 0:1], rstd[:, t:t + 1],
                                            ALU.subtract, ALU.mult).then_inc(xn_ready, 1)

            def x_lo(n):
                t = n % TILES
                dve.wait_ge(xh_ready, n + 1)
                cols = slice(t * P, (t + 1) * P)
                nc.vector.tensor_tensor(xl[:, :, cols], ps_o[n % 2][:, :].rearrange("p (c i) -> p c i", i=P),
                                        xh[:, :, cols].bitcast(F32), ALU.subtract).then_inc(xl_ready, 1)

            def w_lo_chunk(j, c, count, cols=WCOLS):
                dve.wait_ge(w_hi[j], count)
                nc.vector.tensor_tensor(wl[j][:, c, 0:cols], raw[j][:, c, 0:cols],
                                        wh[j][:, c, 0:cols].bitcast(F32), ALU.subtract).then_inc(w_lo[j], 1)

            def phase(g):
                attend, project, goes_out, before = g.flags()
                j = g.half
                prev = 1 - j

                def gated(head, k):
                    m = (j + head) % 2
                    dve.wait_ge(sq_ready, g.times(2, 2 * head + k + 1))
                    dve.wait_ge(proj_ready, g.times(BANKS, BANKS * head + 5 + k))
                    nc.vector.scalar_tensor_tensor(gt[k][:, :], gT[m][:, k * HALF:(k + 1) * HALF], 1.0,
                                                   ps_o[k][:, :], ALU.add, ALU.mult).then_inc(gt_ready, 1)

                def gated_lo(head, k):
                    m = (j + head) % 2
                    cols = slice(k * HALF, (k + 1) * HALF)
                    dve.wait_ge(gh_ready, g.times(2, 2 * head + k + 1))
                    nc.vector.scalar_tensor_tensor(gl[m][:, cols], gt[k][:, :], cst[m][:, NW:NW + 1],
                                                   gh[m][:, cols].bitcast(F32),
                                                   ALU.mult, ALU.subtract).then_inc(gl_ready, 1)

                def add_y(t):
                    if g.reg is None and g.base == 3 and t == 0:
                        dve.wait_ge(yacc_zeroed, 1)
                    dve.wait_ge(y_done, g.pair(TILES, t + 1 - TILES))
                    nc.vector.tensor_tensor(yacc[:, t, :], yacc[:, t, :], ps_vo[:, :], ALU.add).then_inc(y_added, 1)

                for s in range(TILES):
                    if attend:
                        if s == 0:
                            dve.wait_ge(cst_in[prev], g.pair(16, 16 * j))
                        dve.wait_ge(s_done, g.times(TILES, s + 1 - TILES))
                        turns = chunk_buffers(project)
                        _, pss, _, pm = turns[s % len(turns)]
                        nc.vector.tensor_tensor(pm[:, :], pss[:, 0:P], cst[prev][:, MASK:MASK + P],
                                                ALU.mult).then_inc(pm_ready, 1)
                    if goes_out and s >= 1:
                        add_y(s - 1)
                    if before and s == 0:
                        gated(-2, 1)
                    if attend and s == 4:
                        gated(-1, 0)
                    if before and s == 1:
                        gated_lo(-2, 1)
                    if attend and s == 5:
                        gated_lo(-1, 0)
                    if attend and s < KVN:
                        dve.wait_ge(kv_done, g.times(KVN, s + 1 - KVN))
                        if s == 0:
                            nc.vector.tensor_copy(kv[1][:, :], ps_kv[:, 0:HD]).then_inc(kv_ready, 1)
                        else:
                            dve.wait_ge(kv_ready, g.times(KVN, s - KVN))
                            nc.vector.scalar_tensor_tensor(kv[(s + 1) % 2][:, :], kv[s % 2][:, :],
                                                           cst[prev][:, BD:BD + 1], ps_kv[:, 0:HD],
                                                           ALU.mult, ALU.add).then_inc(kv_ready, 1)
                    if s % 2 == 1 and (g.reg is not None or g.base + 1 < LAST):
                        c = s // 2
                        w_lo_chunk(prev, c, g.pair(HC, c + 1 + HC * j))
                if goes_out:
                    add_y(TILES - 1)

            first, second = slice(0, G1), slice(G1, TILES)
            for t in range(G1):
                dve.wait_ge(x_in[t], 16)
                norm_stats(t)
            variances(first)
            normalise(first, 1)
            for t in range(G1):
                dve.wait_ge(x_in[G1 + t], 16)
                norm_stats(G1 + t)
                x_lo(t)
            variances(second)
            normalise(second, 2)
            for t in range(G1, TILES):
                x_lo(t)
            for g in range(FIRST):
                phase(Phase(g))
            with loop(mybir.EngineType.DVE) as r:
                phase(Phase(FIRST, r))
                phase(Phase(FIRST + 1, r))
            for g in (HEADS, HEADS + 1):
                phase(Phase(g))

            dve.wait_ge(rms_done, 1)
            nc.vector.tensor_scalar(var[:, :], ps_t[:, 0:2 * TILES:2], 1.0 / (HEADS * HD), EPS,
                                    ALU.mult, ALU.add).then_inc(var_ready, 1)
            inverse_root(slice(0, TILES), 3, rs)
            nc.vector.tensor_scalar(rs[:, :], rs[:, :], 0.5, None, ALU.mult).then_inc(rs_ready, 1)
            dve.wait_ge(rs_ready, 1)
            dve.wait_ge(wg_hi, 1)
            nc.vector.tensor_tensor(wgl[:, :, :], wg, wgh[:, :, :].bitcast(F32), ALU.subtract).then_inc(wg_lo, 1)

            def x2(t):
                dve.wait_ge(y_done, TILES * (HEADS // 2 - 1) + t + 1)
                dve.wait_ge(y_based, t + 1)
                nc.vector.scalar_tensor_tensor(xs[:, t, :], ps_out[t % 4][:, :], rs[:, t:t + 1], xs[:, t, :],
                                               ALU.mult, ALU.add).then_inc(x2_ready, 1)
                dve.wait_ge(x2_ready, t + 1)

            def choose(k):
                n = TILES // 2
                grid = [P, n, EXPERTS, EXPERTS]
                dve.wait_ge(logit_turned, k + 1)
                link(nc.vector.tensor_copy(lg[:, :, :].rearrange("p t e -> p (t e)"), ps_t[:, 0:n * EXPERTS]))
                other = lg[:, :, :].unsqueeze(2).broadcast_to(grid)
                own = lg[:, :, :].unsqueeze(3).broadcast_to(grid)
                link(nc.vector.tensor_tensor(more[:, :, :, :], other, own, ALU.is_gt))
                link(nc.vector.tensor_tensor(same[:, :, :, :], other, own, ALU.is_equal))
                link(nc.vector.tensor_tensor(same[:, :, :, :], same[:, :, :, :],
                                             tri_sb[:, :, :].unsqueeze(1).broadcast_to(grid), ALU.mult))
                link(nc.vector.tensor_tensor(more[:, :, :, :], more[:, :, :, :], same[:, :, :, :], ALU.add))
                link(nc.vector.tensor_reduce(rank[:, k * n:(k + 1) * n, :], more[:, :, :, :], AX_X, ALU.add))
                nc.vector.tensor_scalar(route[:, :, k * n:(k + 1) * n].rearrange("p e t -> p t e"),
                                        rank[:, k * n:(k + 1) * n, :], TOP_K - 0.5, 1.0 / TOP_K,
                                        ALU.is_lt, ALU.mult).then_inc(routed, 1)

            def add_bias(e, t):
                n = TILES * e + t
                if t == 0:
                    dve.wait_ge(bias_in[e % 2], 16 * (e // 2 + 1))
                dve.wait_ge(f_done, n + 1)
                if n >= 2:
                    dve.wait_ge(relu_ready, n - 1)
                nc.vector.tensor_tensor(z[n % 2][:, :], ps_out[n % 4][:, :], bias[e % 2],
                                        ALU.add).then_inc(z_ready, 1)

            def w_lo_expert(e, c):
                w_lo_chunk(e % 2, c, expert_splits(e) - HC + c + 1, HID)

            for m in range(GROUPS):
                cols = slice(m * G2, (m + 1) * G2)
                for t in range(cols.start, cols.stop):
                    x2(t)
                    norm_stats(t)
                variances(cols)
                if m >= 1:
                    for t in range(cols.start - G2, cols.start):
                        x_lo(TILES + t)
                inverse_root(cols, 4 + m, rstd)
                nc.vector.scalar_tensor_tensor(negm[:, cols], mv[:, cols, 0], -1.0, rstd[:, cols],
                                               ALU.mult, ALU.mult).then_inc(norm_ready, 1)
            for t in range(TILES - G2, TILES):
                x_lo(TILES + t)
            add_bias(0, 0)
            add_bias(0, 1)
            choose(0)
            for t in range(2, 5):
                add_bias(0, t)
                w_lo_expert(1, t - 2)
            choose(1)
            w_lo_expert(1, HC - 1)
            for t in range(5, TILES):
                add_bias(0, t)

            for e in range(1, EXPERTS):
                for t in range(TILES):
                    if t % 2 == 1 and e + 1 < EXPERTS:
                        w_lo_expert(e + 1, t // 2)
                    add_bias(e, t)

        @block.tensor
        def _(pe):
            def three(ps, stat, mov, first, last):
                nc.tensor.matmul(ps, stat[0], mov[1], start=first, stop=False)
                nc.tensor.matmul(ps, stat[0], mov[0], start=False, stop=False)
                return nc.tensor.matmul(ps, stat[1], mov[0], start=False, stop=last)

            def transpose_x(n):
                t = n % TILES
                pe.wait_ge(xn_ready, n + 1)
                if n >= 2:
                    pe.wait_ge(xl_ready, n - 1)
                for c in range(HC):
                    last = nc.tensor.transpose(ps_o[n % 2][:, c * P:(c + 1) * P],
                                               yacc[:, t, c * P:(c + 1) * P], ident[:, :])
                last.then_inc(xt_done, 1)

            def phase(g):
                attend, project, goes_out, before = g.flags()
                j = g.half
                prev = 1 - j
                turns = chunk_buffers(project)

                def scores(s):
                    pst, pss = turns[s % len(turns)][0:2]
                    if s == 1 and not project:
                        pe.wait_ge(proj_ready, BANKS * HEADS)
                    cols = slice(s * P, (s + 1) * P)
                    used = max(s + 1 - len(turns), 0) - TILES
                    need(pe, kn_ready, g.times(TILES, used))
                    nc.tensor.transpose(pst[:, 0:HD], kT[prev][:, cols], ident[:, :]).then_inc(t_done, 1)
                    need(pe, pm_ready, g.times(TILES, used))
                    nc.tensor.matmul(pss[:, 0:P], kT[prev][:, cols], qT[prev][:, cols],
                                     start=True, stop=True).then_inc(s_done, 1)

                for s in range(TILES):
                    tile = slice(s * P, (s + 1) * P)
                    kn, pm = turns[s % len(turns)][2:4]
                    if g.reg is None and g.base == 0 and s == 2:
                        for t in range(G1, TILES):
                            transpose_x(t)
                    if attend:
                        if s % 4 == 0:
                            pe.wait_ge(proj_ready, g.times(BANKS, s // 2 + 2 - BANKS))
                        if project:
                            scores(s)
                        else:
                            for ahead in ((0, 1) if s == 0 else (s + 1,)):
                                if ahead < TILES:
                                    scores(ahead)
                    if project:
                        for n in range(PIECES * s, PIECES * (s + 1)):
                            b, c = n // HC, n % HC
                            what, th = ORDER[b]
                            if g.reg is None and g.base == 0 and c == 0 and b in (0, 2):
                                pe.wait_ge(xl_ready, G1 if b == 0 else TILES)
                            if b == 0:
                                pe.wait_ge(w_lo[j], g.pair(HC, c + 1))
                            if c == 0:
                                need(pe, proj_ready, g.times(BANKS, b - 1))
                            w = slice(COL[what], COL[what] + HD)
                            x0 = slice(th * HALF, (th + 1) * HALF)
                            last = three(ps_proj[b % 2][:, :], (wh[j][:, c, w], wl[j][:, c, w]),
                                         (xh[:, c, x0], xl[:, c, x0]), c == 0, c == HC - 1)
                            if c == HC - 1:
                                last.then_inc(proj_done, 1)
                    if attend:
                        vs = v[:, s, prev * HD:(prev + 1) * HD]
                        if s < KVN:
                            pe.wait_ge(kn_ready, g.times(TILES, s + 1 - TILES))
                            need(pe, kv_ready, g.times(KVN, s - KVN))
                            if s == 1 and j == 1:
                                pe.wait_ge(v_ready, g.pair(TILES, TILES))
                            nc.tensor.matmul(ps_kv[:, 0:HD], kn[:, :], vs, start=True, stop=True).then_inc(kv_done, 1)
                        o = ps_o[s // 4][:, (s % 4) * P:(s % 4 + 1) * P]
                        if s % 4 == 0:
                            need(pe, gt_ready, g.times(2, s // 4 - 3))
                        pe.wait_ge(pm_ready, g.times(TILES, s + 1 - TILES))
                        last = nc.tensor.matmul(o, vs, pm[:, :], start=True, stop=s == 0)
                        if s:
                            pe.wait_ge(kv_ready, g.times(KVN, s - KVN))
                            if s in (1, 4):
                                pe.wait_ge(qd_ready, g.times(2, s // 4 - 1))
                            last = nc.tensor.matmul(o, kv[s % 2][:, :], qdT[prev][:, tile], start=False, stop=True)
                        if s % 4 == 3:
                            last.then_inc(o_done, 1)
                    if project and j == 0:
                        if s == 0:
                            pe.wait_ge(w_lo[0], g.pair(HC, HC))
                            need(pe, y_added, g.pair(TILES, -TILES))
                        else:
                            pe.wait_ge(v_ready, g.pair(TILES, s))
                        for c in range(HC):
                            w = slice(V0, V0 + 2 * HD)
                            last = three(ps_vo[:, 0:2 * HD], (xh[:, c, tile], xl[:, c, tile]),
                                         (wh[0][:, c, w], wl[0][:, c, w]), c == 0, c == HC - 1)
                        last.then_inc(v_done, 1)
                    if goes_out:
                        if s == 0:
                            pe.wait_ge(w_lo[1], g.pair(HC, HC))
                            if project:
                                pe.wait_ge(v_ready, g.pair(TILES, TILES))
                        else:
                            pe.wait_ge(y_added, g.pair(TILES, s - TILES))
                        if s % 4 == 0:
                            pe.wait_ge(gl_ready, g.times(2, s // 4 - 3))
                        for m in range(2):
                            w = slice(V0, V0 + 2 * HD)
                            last = three(ps_vo[:, :].rearrange("p (a b) -> p a b", a=2),
                                         (gh[m][:, tile], gl[m][:, tile]),
                                         (wh[1][:, 2 * m:2 * m + 2, w], wl[1][:, 2 * m:2 * m + 2, w]),
                                         m == 0, m == 1)
                        last.then_inc(y_done, 1)

            pe.wait_ge(ident_made, 2)
            for t in range(G1):
                transpose_x(t)
            for g in range(FIRST):
                phase(Phase(g))
            with loop(mybir.EngineType.PE) as r:
                phase(Phase(FIRST, r))
                phase(Phase(FIRST + 1, r))
            phase(Phase(HEADS))

            def out_tile(t):
                if t == 0:
                    pe.wait_ge(w_lo[1], SPLITS)
                    pe.wait_ge(kv_ready, KVN * HEADS)
                    pe.wait_ge(kn_ready, TILES * HEADS)
                    pe.wait_ge(pm_ready, TILES * HEADS)
                if t % 4 == 0:
                    pe.wait_ge(gl_ready, 2 * HEADS - 1 + t // 4)
                if t >= 4:
                    pe.wait_ge(x2_ready, t - 3)
                tile = slice(t * P, (t + 1) * P)
                w = slice(V0, V0 + 2 * HD)
                for m in range(2):
                    last = three(ps_out[t % 4][:, :].rearrange("p (a b) -> p a b", a=2),
                                 (gh[m][:, tile], gl[m][:, tile]),
                                 (wh[1][:, 2 * m:2 * m + 2, w], wl[1][:, 2 * m:2 * m + 2, w]), m == 0, m == 1)
                last.then_inc(y_done, 1)

            for t in range(2):
                out_tile(t)
            pe.wait_ge(sq_added, 2 * HEADS)
            pe.wait_ge(zeroed, 2)
            pe.wait_ge(kn_ready, HEADS * TILES)
            for t in range(TILES):
                last = nc.tensor.matmul(ps_t[:, 2 * t:2 * t + 2], sqacc[:, t * P:(t + 1) * P], ones[:, :],
                                        start=True, stop=True)
            last.then_inc(rms_done, 1)
            for t in range(2, TILES - 1):
                out_tile(t)

            def expert_tile(e, t):
                n = TILES * e + t
                if t == 0:
                    pe.wait_ge(w_lo[e % 2], expert_splits(e))
                if e == 0:
                    pe.wait_ge(xl_ready, TILES + t + 1)
                if n < 4:
                    pe.wait_ge(x2_ready, TILES - 3 + n)
                else:
                    pe.wait_ge(z_ready, n - 3)
                for c in range(HC):
                    tile = slice(t * P, (t + 1) * P)
                    last = three(ps_out[n % 4][:, :], (xh[:, c, tile], xl[:, c, tile]),
                                 (wh[e % 2][:, c, 0:HID], wl[e % 2][:, c, 0:HID]), c == 0, c == HC - 1)
                last.then_inc(f_done, 1)

            def logits(k):
                if k == 0:
                    pe.wait_ge(wg_lo, 1)
                    pe.wait_ge(pm_ready, HEADS * TILES)
                pe.wait_ge(xl_ready, TILES + (k + 1) * TILES // 2)
                if k:
                    pe.wait_ge(logit_ready, k)
                half = slice(k * HALF, (k + 1) * HALF)
                for c in range(HC):
                    last = three(ps_s[:, :], (wgh[:, c, :], wgl[:, c, :]), (xh[:, c, half], xl[:, c, half]),
                                 c == 0, c == HC - 1)
                last.then_inc(logit_done, 1)

            def turn_logits(k):
                pe.wait_ge(logit_ready, k + 1)
                if k:
                    pe.wait_ge(routed, k)
                for m in range(TILES // 2):
                    last = nc.tensor.transpose(ps_t[:, EXPERTS * m:EXPERTS * (m + 1)],
                                               lgT[:, k * HALF + m * P:k * HALF + (m + 1) * P],
                                               ident[0:EXPERTS, 0:EXPERTS])
                last.then_inc(logit_turned, 1)

            for t in range(2):
                transpose_x(TILES + t)
            out_tile(TILES - 1)
            for t in range(2, 4):
                transpose_x(TILES + t)
            expert_tile(0, 0)
            transpose_x(TILES + 4)
            expert_tile(0, 1)
            transpose_x(TILES + 5)
            logits(0)
            transpose_x(TILES + 6)
            expert_tile(0, 2)
            transpose_x(TILES + 7)
            turn_logits(0)
            for t in (3, 4, 5):
                expert_tile(0, t)
            logits(1)
            expert_tile(0, 6)
            turn_logits(1)
            expert_tile(0, 7)
            for e in range(1, EXPERTS):
                for t in range(TILES):
                    expert_tile(e, t)


def head_constants():
    layer_idx, n_layers = 1, 32
    base = 1.0 / 2.0 ** (8.0 / HEADS)
    factor = 1.0 - layer_idx / (n_layers - 1 + 1e-05) + 1e-05
    slope = (base ** (np.arange(HEADS) + 1.0) * factor)[:, None, None]
    r = np.arange(P) + 1.0
    diff = r[None, :] - r[:, None]
    mask = np.where(diff >= 0, np.exp(-slope * np.maximum(diff, 0)), 0.0)
    qd = np.broadcast_to(np.exp(-slope * r), (HEADS, P, P))
    kd = np.exp(-slope * (P - r)[:, None])
    bd = np.broadcast_to(np.exp(-slope * P), (HEADS, P, 1))
    return np.concatenate([mask, qd, kd, bd], axis=2).astype(np.float32)


def kernel(**inputs):
    import concourse.bacc as bacc
    from concourse.bass_utils import run_bass_kernel_spmd

    a = {k.split("_", 1)[1]: np.asarray(val) for k, val in inputs.items()}
    x = np.ascontiguousarray(a["attn_hidden_states"]).reshape(TOKENS, HID)

    def transposed(w):
        return w.T.reshape(HC, P, -1).transpose(1, 0, 2)

    qkv = a["attn_qkv_w"].reshape(HEADS, 3, HD, HID)
    gate = a["attn_gate_w"].reshape(HEADS, HD, HID)
    out_w = a["attn_out_w"]
    weights = np.zeros((LAST, P, HC, WCOLS), np.float32)
    for g in range(LAST):
        if g < HEADS:
            weights[g, :, :, 0:HD] = transposed(qkv[g, 0])
            weights[g, :, :, HD:2 * HD] = transposed(qkv[g, 1])
            weights[g, :, :, 2 * HD:3 * HD] = transposed(gate[g])
            if g % 2 == 0:
                weights[g, :, :, V0:V0 + HD] = transposed(qkv[g, 2])
                weights[g, :, :, V0 + HD:V0 + 2 * HD] = transposed(qkv[g + 1, 2])
        if g % 2 == 1 and g >= 3:
            for m in range(2):
                h = g - 3 + m
                w = out_w[:, h * HD:(h + 1) * HD].T
                weights[g, :, 2 * m:2 * m + 2, V0:V0 + 2 * HD] = w.reshape(HD, 2, 2 * HD)
    experts = a["ffn_W_e"].reshape(EXPERTS, HC, P, HID).transpose(0, 2, 1, 3)
    weights[HEADS, :, :, 0:HID] = experts[0]
    w_gate = np.zeros((P, HC, P), np.float32)
    w_gate[:, :, 0:EXPERTS] = a["ffn_W_gate"].reshape(HC, P, EXPERTS).transpose(1, 0, 2)
    norm_w = a["attn_norm_w"].reshape(HEADS, HD, 1)
    consts = np.concatenate([head_constants(), norm_w], axis=2)
    tri = np.broadcast_to(np.tril(np.ones((EXPERTS, EXPERTS), np.float32), -1), (P, EXPERTS, EXPERTS))

    arrays = {
        "x": x, "weights": weights, "experts": experts, "head_consts": consts,
        "w_gate": w_gate, "b_gate": a["ffn_b_gate"].reshape(EXPERTS, 1),
        "b_exp": a["ffn_b_e"].reshape(EXPERTS, 1, HID),
        "tri": tri,
    }
    arrays = {k: np.ascontiguousarray(val) for k, val in arrays.items()}
    nc = bacc.Bacc("TRN2", target_bir_lowering=False, num_devices=1)
    aps = [nc.dram_tensor(k, val.shape, F32, kind="ExternalInput").ap() for k, val in arrays.items()]
    out = nc.dram_tensor("out", (TOKENS, HID), F32, kind="ExternalOutput").ap()
    layer(nc, *aps, out)
    r = run_bass_kernel_spmd(nc, [arrays], core_ids=[0])
    return r.results[0]["out"].reshape(1, TOKENS, HID)
```
